# Optimizing a Trainium2 kernel written in Bass

```python
import numpy as np
import jax
import jax.numpy as jnp

def _softmax(x, axis=-1):
    return jax.nn.softmax(x, axis=axis)

def _gelu(x):
    return jax.nn.gelu(x, approximate=True)

def _silu(x):
    return jax.nn.silu(x)

def _sigmoid(x):
    return jax.nn.sigmoid(x)

def _layernorm(x, axis=-1, eps=1e-05):
    m = jnp.mean(x, axis=axis, keepdims=True)
    v = jnp.var(x, axis=axis, keepdims=True)
    return (x - m) / jnp.sqrt(v + eps)

def _scatter_add(tgt, idx, src, axis=0):
    return tgt.at[idx].add(src)

def _segment_sum(src, seg, n):
    return jax.ops.segment_sum(src, seg, n)
kernel_name = 'mk_dlrm_tower_d1_rec_r8_8ad175'

def setup_inputs(seed: int=0):
    np.random.seed(seed)
    _w = jnp.asarray

    def _rec_inputs():
        import jax
        import jax.numpy as jnp
        _tk = jax.random.key(seed)
        dense_ctx = jax.random.normal(jax.random.fold_in(_tk, 190), (1024, 16), jnp.float32)
        ids = jnp.stack([jax.random.randint(jax.random.fold_in(_tk, 200 + f), (1024,), 0, v, jnp.int32) for f, v in enumerate([12500, 125000, 125000, 1250, 1250, 1250, 1250, 1250, 12500, 125000, 12500, 12500, 1250, 1000, 1250, 12500, 12500, 125000, 125000, 125000, 1000, 1000, 125000, 1250, 125000, 1000, 12500, 125000, 125000, 125000, 125000, 1250, 1250, 1250, 1000, 1250, 1250, 125000, 125000])], axis=1)
        tbl_0 = 0.05 * jax.random.normal(jax.random.fold_in(_tk, 500 + 0), (12500, 16), jnp.float32)
        tbl_1 = 0.05 * jax.random.normal(jax.random.fold_in(_tk, 500 + 1), (125000, 16), jnp.float32)
        tbl_2 = 0.05 * jax.random.normal(jax.random.fold_in(_tk, 500 + 2), (125000, 16), jnp.float32)
        tbl_3 = 0.05 * jax.random.normal(jax.random.fold_in(_tk, 500 + 3), (1250, 16), jnp.float32)
        tbl_4 = 0.05 * jax.random.normal(jax.random.fold_in(_tk, 500 + 4), (1250, 16), jnp.float32)
        tbl_5 = 0.05 * jax.random.normal(jax.random.fold_in(_tk, 500 + 5), (1250, 16), jnp.float32)
        tbl_6 = 0.05 * jax.random.normal(jax.random.fold_in(_tk, 500 + 6), (1250, 16), jnp.float32)
        tbl_7 = 0.05 * jax.random.normal(jax.random.fold_in(_tk, 500 + 7), (1250, 16), jnp.float32)
        tbl_8 = 0.05 * jax.random.normal(jax.random.fold_in(_tk, 500 + 8), (12500, 16), jnp.float32)
        tbl_9 = 0.05 * jax.random.normal(jax.random.fold_in(_tk, 500 + 9), (125000, 16), jnp.float32)
        tbl_10 = 0.05 * jax.random.normal(jax.random.fold_in(_tk, 500 + 10), (12500, 16), jnp.float32)
        tbl_11 = 0.05 * jax.random.normal(jax.random.fold_in(_tk, 500 + 11), (12500, 16), jnp.float32)
        tbl_12 = 0.05 * jax.random.normal(jax.random.fold_in(_tk, 500 + 12), (1250, 16), jnp.float32)
        tbl_13 = 0.05 * jax.random.normal(jax.random.fold_in(_tk, 500 + 13), (1000, 16), jnp.float32)
        tbl_14 = 0.05 * jax.random.normal(jax.random.fold_in(_tk, 500 + 14), (1250, 16), jnp.float32)
        tbl_15 = 0.05 * jax.random.normal(jax.random.fold_in(_tk, 500 + 15), (12500, 16), jnp.float32)
        tbl_16 = 0.05 * jax.random.normal(jax.random.fold_in(_tk, 500 + 16), (12500, 16), jnp.float32)
        tbl_17 = 0.05 * jax.random.normal(jax.random.fold_in(_tk, 500 + 17), (125000, 16), jnp.float32)
        tbl_18 = 0.05 * jax.random.normal(jax.random.fold_in(_tk, 500 + 18), (125000, 16), jnp.float32)
        tbl_19 = 0.05 * jax.random.normal(jax.random.fold_in(_tk, 500 + 19), (125000, 16), jnp.float32)
        tbl_20 = 0.05 * jax.random.normal(jax.random.fold_in(_tk, 500 + 20), (1000, 16), jnp.float32)
        tbl_21 = 0.05 * jax.random.normal(jax.random.fold_in(_tk, 500 + 21), (1000, 16), jnp.float32)
        tbl_22 = 0.05 * jax.random.normal(jax.random.fold_in(_tk, 500 + 22), (125000, 16), jnp.float32)
        tbl_23 = 0.05 * jax.random.normal(jax.random.fold_in(_tk, 500 + 23), (1250, 16), jnp.float32)
        tbl_24 = 0.05 * jax.random.normal(jax.random.fold_in(_tk, 500 + 24), (125000, 16), jnp.float32)
        tbl_25 = 0.05 * jax.random.normal(jax.random.fold_in(_tk, 500 + 25), (1000, 16), jnp.float32)
        tbl_26 = 0.05 * jax.random.normal(jax.random.fold_in(_tk, 500 + 26), (12500, 16), jnp.float32)
        tbl_27 = 0.05 * jax.random.normal(jax.random.fold_in(_tk, 500 + 27), (125000, 16), jnp.float32)
        tbl_28 = 0.05 * jax.random.normal(jax.random.fold_in(_tk, 500 + 28), (125000, 16), jnp.float32)
        tbl_29 = 0.05 * jax.random.normal(jax.random.fold_in(_tk, 500 + 29), (125000, 16), jnp.float32)
        tbl_30 = 0.05 * jax.random.normal(jax.random.fold_in(_tk, 500 + 30), (125000, 16), jnp.float32)
        tbl_31 = 0.05 * jax.random.normal(jax.random.fold_in(_tk, 500 + 31), (1250, 16), jnp.float32)
        tbl_32 = 0.05 * jax.random.normal(jax.random.fold_in(_tk, 500 + 32), (1250, 16), jnp.float32)
        tbl_33 = 0.05 * jax.random.normal(jax.random.fold_in(_tk, 500 + 33), (1250, 16), jnp.float32)
        tbl_34 = 0.05 * jax.random.normal(jax.random.fold_in(_tk, 500 + 34), (1000, 16), jnp.float32)
        tbl_35 = 0.05 * jax.random.normal(jax.random.fold_in(_tk, 500 + 35), (1250, 16), jnp.float32)
        tbl_36 = 0.05 * jax.random.normal(jax.random.fold_in(_tk, 500 + 36), (1250, 16), jnp.float32)
        tbl_37 = 0.05 * jax.random.normal(jax.random.fold_in(_tk, 500 + 37), (125000, 16), jnp.float32)
        tbl_38 = 0.05 * jax.random.normal(jax.random.fold_in(_tk, 500 + 38), (125000, 16), jnp.float32)
        _rk = jax.random.fold_in(_tk, 7)
        W_top1 = 0.05 * jax.random.normal(jax.random.fold_in(_tk, 801), (400, 512), jnp.float32)
        W_top2 = 0.0441942 * jax.random.normal(jax.random.fold_in(_tk, 802), (512, 256), jnp.float32)
        W_top3 = 0.0625 * jax.random.normal(jax.random.fold_in(_tk, 803), (256, 1), jnp.float32)
        b_top1 = jnp.zeros((512,), jnp.float32)
        b_top2 = jnp.zeros((256,), jnp.float32)
        return (dense_ctx, ids, tbl_0, tbl_1, tbl_2, tbl_3, tbl_4, tbl_5, tbl_6, tbl_7, tbl_8, tbl_9, tbl_10, tbl_11, tbl_12, tbl_13, tbl_14, tbl_15, tbl_16, tbl_17, tbl_18, tbl_19, tbl_20, tbl_21, tbl_22, tbl_23, tbl_24, tbl_25, tbl_26, tbl_27, tbl_28, tbl_29, tbl_30, tbl_31, tbl_32, tbl_33, tbl_34, tbl_35, tbl_36, tbl_37, tbl_38, W_top1, b_top1, W_top2, b_top2, W_top3)
    dense_ctx, ids, tbl_0, tbl_1, tbl_2, tbl_3, tbl_4, tbl_5, tbl_6, tbl_7, tbl_8, tbl_9, tbl_10, tbl_11, tbl_12, tbl_13, tbl_14, tbl_15, tbl_16, tbl_17, tbl_18, tbl_19, tbl_20, tbl_21, tbl_22, tbl_23, tbl_24, tbl_25, tbl_26, tbl_27, tbl_28, tbl_29, tbl_30, tbl_31, tbl_32, tbl_33, tbl_34, tbl_35, tbl_36, tbl_37, tbl_38, W_top1, b_top1, W_top2, b_top2, W_top3 = _rec_inputs()

    def _L0_rec_setup():
        import jax, jax.numpy as jnp
        import numpy as np
        B, F0, D = (256, 39, 16)
        CROSS = [128, 128, 128]
        key = jax.random.key(seed)
        k0, k1, k2, k3 = jax.random.split(key, 4)
        inputs = jax.random.normal(k0, (B, F0, D), dtype=jnp.float32)
        f0 = jax.random.normal(k1, (F0 * F0, CROSS[0]), dtype=jnp.float32) * 0.05
        f1 = jax.random.normal(k2, (CROSS[0] * F0, CROSS[1]), dtype=jnp.float32) * 0.05
        f2 = jax.random.normal(k3, (CROSS[1] * F0, CROSS[2]), dtype=jnp.float32) * 0.05
        return {'inputs': inputs, 'f0': f0, 'f1': f1, 'f2': f2}
    _L0_rec_all = _L0_rec_setup()
    _L0_rec_in = {k: v for k, v in _L0_rec_all.items() if k in ('f0', 'f1', 'f2')}
    del _L0_rec_all
    return {'dense_ctx': dense_ctx, 'ids': ids, 'tbl_0': tbl_0, 'tbl_1': tbl_1, 'tbl_2': tbl_2, 'tbl_3': tbl_3, 'tbl_4': tbl_4, 'tbl_5': tbl_5, 'tbl_6': tbl_6, 'tbl_7': tbl_7, 'tbl_8': tbl_8, 'tbl_9': tbl_9, 'tbl_10': tbl_10, 'tbl_11': tbl_11, 'tbl_12': tbl_12, 'tbl_13': tbl_13, 'tbl_14': tbl_14, 'tbl_15': tbl_15, 'tbl_16': tbl_16, 'tbl_17': tbl_17, 'tbl_18': tbl_18, 'tbl_19': tbl_19, 'tbl_20': tbl_20, 'tbl_21': tbl_21, 'tbl_22': tbl_22, 'tbl_23': tbl_23, 'tbl_24': tbl_24, 'tbl_25': tbl_25, 'tbl_26': tbl_26, 'tbl_27': tbl_27, 'tbl_28': tbl_28, 'tbl_29': tbl_29, 'tbl_30': tbl_30, 'tbl_31': tbl_31, 'tbl_32': tbl_32, 'tbl_33': tbl_33, 'tbl_34': tbl_34, 'tbl_35': tbl_35, 'tbl_36': tbl_36, 'tbl_37': tbl_37, 'tbl_38': tbl_38, 'W_top1': W_top1, 'b_top1': b_top1, 'W_top2': W_top2, 'b_top2': b_top2, 'W_top3': W_top3, 'L0_rec_f0': _L0_rec_in['f0'], 'L0_rec_f1': _L0_rec_in['f1'], 'L0_rec_f2': _L0_rec_in['f2']}

def reference(dense_ctx, ids, tbl_0, tbl_1, tbl_2, tbl_3, tbl_4, tbl_5, tbl_6, tbl_7, tbl_8, tbl_9, tbl_10, tbl_11, tbl_12, tbl_13, tbl_14, tbl_15, tbl_16, tbl_17, tbl_18, tbl_19, tbl_20, tbl_21, tbl_22, tbl_23, tbl_24, tbl_25, tbl_26, tbl_27, tbl_28, tbl_29, tbl_30, tbl_31, tbl_32, tbl_33, tbl_34, tbl_35, tbl_36, tbl_37, tbl_38, W_top1, b_top1, W_top2, b_top2, W_top3, L0_rec_f0, L0_rec_f1, L0_rec_f2):
    import jax
    import jax.numpy as jnp

    def _L0_rec_ref(inputs, f0, f1, f2):
        import jax, jax.numpy as jnp
        import numpy as np
        B, F0, D = (256, 39, 16)
        CROSS = [128, 128, 128]
        filters = [f0, f1, f2]
        x0 = inputs
        xk = inputs
        outs = []
        for W in filters:
            b, f, d = x0.shape
            g = xk.shape[1]
            z = jnp.einsum('bfd,bgd->bfgd', x0, xk).reshape(b, f * g, d)
            cur = jnp.einsum('bpd,pm->bmd', z, W)
            outs.append(cur)
            xk = cur
        result = jnp.concatenate(outs, axis=1)
        return jnp.sum(result, axis=-1)
    e = jnp.stack([tbl_0[ids[:, 0]], tbl_1[ids[:, 1]], tbl_2[ids[:, 2]], tbl_3[ids[:, 3]], tbl_4[ids[:, 4]], tbl_5[ids[:, 5]], tbl_6[ids[:, 6]], tbl_7[ids[:, 7]], tbl_8[ids[:, 8]], tbl_9[ids[:, 9]], tbl_10[ids[:, 10]], tbl_11[ids[:, 11]], tbl_12[ids[:, 12]], tbl_13[ids[:, 13]], tbl_14[ids[:, 14]], tbl_15[ids[:, 15]], tbl_16[ids[:, 16]], tbl_17[ids[:, 17]], tbl_18[ids[:, 18]], tbl_19[ids[:, 19]], tbl_20[ids[:, 20]], tbl_21[ids[:, 21]], tbl_22[ids[:, 22]], tbl_23[ids[:, 23]], tbl_24[ids[:, 24]], tbl_25[ids[:, 25]], tbl_26[ids[:, 26]], tbl_27[ids[:, 27]], tbl_28[ids[:, 28]], tbl_29[ids[:, 29]], tbl_30[ids[:, 30]], tbl_31[ids[:, 31]], tbl_32[ids[:, 32]], tbl_33[ids[:, 33]], tbl_34[ids[:, 34]], tbl_35[ids[:, 35]], tbl_36[ids[:, 36]], tbl_37[ids[:, 37]], tbl_38[ids[:, 38]]], axis=1)
    z = _L0_rec_ref(e, L0_rec_f0, L0_rec_f1, L0_rec_f2)
    z = z.reshape(z.shape[0], -1)
    h = jnp.concatenate([z, dense_ctx], axis=1)
    h = jnp.maximum(h @ W_top1 + b_top1, 0.0)
    h = jnp.maximum(h @ W_top2 + b_top2, 0.0)
    y = h @ W_top3
    return y

_drawn_inputs = setup_inputs


def setup_inputs(seed=0):
    import zlib

    import numpy as np

    out = dict(_drawn_inputs(seed))
    spreads = {'b_top1': (0.0, 0.538), 'b_top2': (0.0, 0.1)}
    factors = {'tbl_0': 4.306,
     'tbl_1': 4.823,
     'tbl_2': 4.381,
     'tbl_3': 4.716,
     'tbl_4': 4.804,
     'tbl_5': 4.871,
     'tbl_6': 4.808,
     'tbl_7': 4.661,
     'tbl_8': 4.846,
     'tbl_9': 4.362,
     'tbl_10': 5.03,
     'tbl_11': 4.677,
     'tbl_12': 4.305,
     'tbl_13': 4.265,
     'tbl_14': 4.706,
     'tbl_15': 4.722,
     'tbl_16': 5.013,
     'tbl_17': 4.629,
     'tbl_18': 5.098,
     'tbl_19': 5.06,
     'tbl_20': 5.049,
     'tbl_21': 4.778,
     'tbl_22': 4.655,
     'tbl_23': 4.808,
     'tbl_24': 4.325,
     'tbl_25': 4.446,
     'tbl_26': 4.833,
     'tbl_27': 4.941,
     'tbl_28': 4.747,
     'tbl_29': 4.831,
     'tbl_30': 4.837,
     'tbl_31': 4.334,
     'tbl_32': 4.696,
     'tbl_33': 4.876,
     'tbl_34': 4.776,
     'tbl_35': 4.48,
     'tbl_36': 4.864,
     'tbl_37': 4.775,
     'tbl_38': 4.77,
     'L0_rec_f1': 4.963,
     'L0_rec_f2': 8.0}
    for name, (base, spread) in spreads.items():
        noise = np.random.default_rng([zlib.crc32(name.encode()), seed]).standard_normal(out[name].shape)
        drawn = base * np.exp(spread * noise) if base else spread * noise
        out[name] = jnp.asarray(drawn.astype(out[name].dtype))
    for name, factor in factors.items():
        out[name] = (out[name] * factor).astype(out[name].dtype)
    return out
```

```python
from contextlib import ExitStack

import concourse.bass as bass
from concourse import mybir

F32 = mybir.dt.float32
F32R = mybir.dt.float32r
I32 = mybir.dt.int32
ALU = mybir.AluOpType
ACT = mybir.ActivationFunctionType
AX = mybir.AxisListType

P = 128
B, NF, D = 1024, 39, 16
M = 128
BT = B // P
QG = 4
GB = P // QG
GN = GB * D
JT = GN // P
TB = P // D
TPB = QG * JT
FC = NF + 1

SHIFTS = NF // 2 + 1
SPK = P // NF
K0 = -(-SHIFTS // SPK)
K0_ROWS = [NF * min(SPK, SHIFTS - SPK * k) for k in range(K0)]
SEL = SPK * NF

CH = -(-NF // 4)
CH_F = [range(4 * c, min(4 * c + 4, NF)) for c in range(CH)]
FUSED = (3, 6, 9)
SCALED = tuple(c for c in range(CH) if c not in FUSED)
YB = 4
PR = 3
SLOTS = JT * CH

AT_FIELDS, AT_SCALARS = 4, 5
AT_PAIR = [6 + 4 * k for k in range(K0)]
AT_SUM = [10 + 4 * k for k in range(K0)]
AT_SPLIT = 35
AT_G, AT_GREAD = 7, 8
L2_PARTS = 3
L2_F = NF // L2_PARTS
GATHERS = 3
GATHER_FROM = 11
EARLY = GATHERS * (TPB - GATHER_FROM)


def vector_steps():
    steps, held = [], None
    for c in range(CH):
        if c in FUSED:
            steps += [("fuse", c, i) for i in range(len(CH_F[c]))]
        if held is not None:
            steps.append(("add", held, 0))
            held = None
        if c in SCALED[1:]:
            held = c
    return steps


STEPS = vector_steps()
NST = len(STEPS)
STEP_DONE = {c: max(n for n, s in enumerate(STEPS) if s[1] == c) + 1 for _, c, _ in STEPS}
NSC = len(SCALED)

FILLS_G = 2 + K0
FILLS = QG + QG * FILLS_G
ACT_READS = QG + 2 * QG
DVE_READS = K0 * QG


def fill_reader(n):
    if n < QG:
        return False, n + 1
    q, r = divmod(n - QG, FILLS_G)
    return (False, QG + 2 * q + r + 1) if r < 2 else (True, K0 * q + r - 1)


def build(nc, dense, ids, tables, w1, b1, w2, b2, w3, f0, f1, f2, out):
    ctx = ExitStack()
    with ctx:
        def sb(name, shape, dt=F32):
            return ctx.enter_context(nc.sbuf_tensor(name, shape, dt))

        def ps(name):
            return ctx.enter_context(nc.psum_tensor(name, [P, 512], F32))

        def sem(name):
            return ctx.enter_context(nc.semaphore(name))

        f1_high = sb("f1_high", [P, NF, M], F32R)
        f1_low = sb("f1_low", [P, NF, M], F32R)
        f2_sb = sb("f2_sb", [P, NF, M])
        f0_sum = sb("f0_sum", [SEL, K0, M])
        f0_mirror = sb("f0_mirror", [SEL, K0, M])
        w1_sb = sb("w1_sb", [P, 3, 512])
        w1_dense = sb("w1_dense", [D, 512])
        w2_sb = sb("w2_sb", [P, 4, 256])
        w3_sb = sb("w3_sb", [P, 2])
        b1_sb = sb("b1_sb", [P, 4])
        b2_sb = sb("b2_sb", [P, 2])
        ident = sb("ident", [P, P])
        ident_r = sb("ident_r", [P, P], F32R)
        comb = sb("comb", [2 * NF, 2 * NF])
        comb_r = sb("comb_r", [2 * NF, FC], F32R)
        select = sb("select", [2 * NF, 1 + K0, SEL], F32R)
        block = sb("block", [P, TB])
        ids_sb = sb("ids_sb", [P, BT, NF], I32)
        ids_now = sb("ids_now", [P, NF], I32)
        rows = sb("rows", [P, NF * D])
        rows_parts = sb("rows_parts", [P, D, 2, NF], F32R)
        x_parts = sb("x_parts", [2 * NF, P, D], F32R)
        fields = sb("fields", [SEL, GN])
        pairs = sb("pairs", [SEL, 2, GN])
        cur0_high = sb("cur0_high", [P, 2, GN], F32R)
        cur0_low = sb("cur0_low", [P, 2, GN], F32R)
        x_col = sb("x_col", [P, 2, JT, FC])
        scaled_sb = sb("scaled_sb", [P, PR, 4 * M])
        acc_s = sb("acc_s", [P, 2, 4 * M])
        acc_f = sb("acc_f", [P, 2, 2 * M])
        fold_a = sb("fold_a", [P, 2 * M])
        fold_b = sb("fold_b", [P, 2 * M])
        cur1 = sb("cur1", [P, 2, M])
        x_block = sb("x_block", [P, 2, JT, TB * FC])
        G = sb("G", [P, 2 * FC * P])
        f1_raw = G[:, 0:NF * M]
        h1 = G[:, 0:4 * B].rearrange("p (m b) -> p m b", m=4)
        z0, z1, z2 = sb("z0", [P, B]), sb("z1", [P, B]), sb("z2", [P, B])
        dense_sb = sb("dense_sb", [P, BT, D])
        z_dense = sb("z_dense", [D, B])
        h2 = sb("h2", [P, 2, 512])
        y = sb("y", [1, B])

        Y = [ps(f"Y{i}") for i in range(YB)]
        X = [ps("X0"), ps("X1")]
        C = ps("C")
        GP = ps("GP")

        ids_in, ids_ready, gathered = sem("ids_in"), sem("ids_ready"), sem("gathered")
        consts_made, sel_ready, block_ready = sem("consts_made"), sem("sel_ready"), sem("block_ready")
        mirror_zero, f0_in, f0_ready = sem("mirror_zero"), sem("f0_in"), sem("f0_ready")
        f1_in, f1_high_ready, f1_ready = [sem(f"f1_in{i}") for i in range(3)], sem("f1_high_ready"), sem("f1_ready")
        f2_in, dense_in, mlp_in = sem("f2_in"), sem("dense_in"), sem("mlp_in")
        dense_filled, dense_read = sem("dense_filled"), sem("dense_read")
        rows_high_ready, rows_split = sem("rows_high_ready"), sem("rows_split")
        x_filled, x_read, pairs_ready = sem("x_filled"), sem("x_read"), sem("pairs_ready")
        cur0_summed, cur0_high_ready, cur0_ready, cur0_read = (
            sem("cur0_summed"), sem("cur0_high_ready"), sem("cur0_ready"), sem("cur0_read"))
        y_filled, scaled, acc_steps, folds = sem("y_filled"), sem("scaled"), sem("acc_steps"), sem("folds")
        ones_set, block_made = sem("ones_set"), sem("block_made")
        g_filled, g_read = sem("g_filled"), sem("g_read")
        l2_filled, l2_read, z1_copied = sem("l2_filled"), sem("l2_read"), sem("z1_copied")
        m1_filled, m1_read, m2_filled, m2_read, m3_filled, m3_read = (
            sem("m1_filled"), sem("m1_read"), sem("m2_filled"), sem("m2_read"), sem("m3_filled"), sem("m3_read"))
        y_out = sem("y_out")

        f1_cuts = [13, 26, 39]

        def f0_pieces():
            for s in range(SHIFTS):
                k, p0 = divmod(s, SPK)
                p0 *= NF
                whole = NF - s
                yield False, k, p0, whole, s, NF + 1
                if s:
                    yield False, k, p0 + whole, s, whole * NF, NF + 1
                    yield True, k, p0, whole, NF * s, NF + 1
                    yield True, k, p0 + whole, s, whole, NF + 1

        pieces = list(f0_pieces())

        def load_f0(eng, which):
            for mirror, k, p0, n, first, step in which:
                dst = (f0_mirror if mirror else f0_sum)[p0:p0 + n, k, :]
                eng.dma_start(dst, f0[first:first + step * (n - 1) + 1:step, :]).then_inc(f0_in, 16)

        def column_tile(bt, q, j):
            return TPB * bt + JT * q + j

        blk = ctx.enter_context(nc.Block())

        @blk.sync
        def _(sp):
            sp.dma_start(ids_sb[:], ids.rearrange("(t p) f -> p t f", p=P)).then_inc(ids_in, 16)
            load_f0(sp, pieces[0::2])
            lo = 0
            for i, hi in enumerate(f1_cuts):
                sp.dma_start(f1_raw[:, lo * M:hi * M].rearrange("p (f m) -> p f m", m=M),
                             f1.rearrange("(f g) m -> g f m", g=M)[:, lo:hi, :]).then_inc(f1_in[i], 16)
                lo = hi
            sp.dma_start(dense_sb[:], dense.rearrange("(t p) c -> p t c", p=P)).then_inc(dense_in, 16)
            sp.dma_start(f2_sb[:], f2.rearrange("(f g) m -> g f m", g=M)).then_inc(f2_in, 16)
            sp.dma_start(w1_sb[:], w1[0:3 * P, :].rearrange("(k p) n -> p k n", p=P)).then_inc(mlp_in, 16)
            sp.dma_start(w1_dense[:], w1[3 * P:3 * P + D, :]).then_inc(mlp_in, 16)
            sp.dma_start(w2_sb[:], w2.rearrange("(k p) n -> p k n", p=P)).then_inc(mlp_in, 16)
            sp.dma_start(w3_sb[:], w3.rearrange("(k p) o -> p (k o)", p=P),
                         allow_slow_non_contiguous=True).then_inc(mlp_in, 16)
            sp.dma_start(b1_sb[:], b1.rearrange("(m p) -> p m", p=P),
                         allow_slow_non_contiguous=True).then_inc(mlp_in, 16)
            sp.dma_start(b2_sb[:], b2.rearrange("(m p) -> p m", p=P),
                         allow_slow_non_contiguous=True).then_inc(mlp_in, 16)
            sp.wait_ge(m3_read, 2)
            sp.dma_start(out.rearrange("b o -> o b"), y[:]).then_inc(y_out, 16)
            sp.wait_ge(y_out, 16)

        @blk.gpsimd
        def _(pool):
            pool.memset(ident[:], 0.0).then_inc(consts_made, 1)
            pool.memset(comb[:], 0.0).then_inc(consts_made, 1)
            pool.memset(block[:], 1.0).then_inc(consts_made, 1)
            pool.wait_ge(consts_made, 3)
            pool.affine_select(out=ident[:], in_=ident[:], compare_op=ALU.not_equal, fill=1.0, base=0,
                               pattern=[[-1, P]], channel_multiplier=1).then_inc(consts_made, 1)
            for i, off in enumerate((0, NF, -NF)):
                if i:
                    pool.wait_ge(consts_made, 4 + i)
                pool.affine_select(out=comb[:], in_=comb[:], compare_op=ALU.not_equal, fill=1.0, base=off,
                                   pattern=[[-1, 2 * NF]], channel_multiplier=1).then_inc(consts_made, 1)
            pool.affine_select(out=block[:], in_=block[:], compare_op=ALU.is_ge, fill=0.0, base=0,
                               pattern=[[-D, TB]], channel_multiplier=1).then_inc(block_ready, 1)
            pool.wait_ge(block_ready, 1)
            pool.affine_select(out=block[:], in_=block[:], compare_op=ALU.is_ge, fill=0.0, base=D - 1,
                               pattern=[[D, TB]], channel_multiplier=-1).then_inc(block_ready, 1)

            def take_ids(bt):
                pool.tensor_copy(ids_now[:], ids_sb[:, bass.ds(bt, 1), :].rearrange("p o f -> p (o f)"))\
                    .then_inc(ids_ready, 1)

            def gather(fs):
                for f in fs:
                    pool.indirect_dma_start(
                        out=rows[:, f * D:(f + 1) * D], out_offset=None, in_=tables[f],
                        in_offset=bass.IndirectOffsetOnAxis(ap=ids_now[:, f:f + 1], axis=0),
                    ).then_inc(gathered, 16)

            def spread(bt, q):
                group = QG * bt + q
                pool.wait_ge(x_read, ACT_READS * bt + fill_reader(QG + FILLS_G * q + 1)[1])
                if not (isinstance(bt, int) and QG * bt + q < 2):
                    pool.wait_ge(g_filled, JT * (group - 1))
                for j in range(JT):
                    ins = pool.tensor_tensor(
                        x_block[:, q % 2, j, :].rearrange("p (b f) -> p b f", b=TB),
                        x_col[:, q % 2, j, :].unsqueeze(1).broadcast_to([P, TB, FC]),
                        block[:].unsqueeze(2).broadcast_to([P, TB, FC]), ALU.mult)
                ins.then_inc(block_made, 1)

            def fold(bt, q, j):
                t = column_tile(bt, q, j)
                pool.wait_ge(acc_steps, NST * (t + 1))
                a, f = acc_s[:, j % 2, :], acc_f[:, j % 2, :]
                pool.tensor_tensor(fold_a[:], a[:, 0:2 * M], a[:, 2 * M:4 * M], ALU.add).then_inc(folds, 1)
                pool.wait_ge(folds, 3 * t + 1)
                pool.tensor_tensor(fold_b[:], fold_a[:], f, ALU.add).then_inc(folds, 1)
                pool.wait_ge(folds, 3 * t + 2)
                if not (isinstance(t, int) and t < 2):
                    pool.wait_ge(g_filled, t - 1)
                pool.tensor_tensor(cur1[:, j % 2, :], fold_b[:, 0:M], fold_b[:, M:2 * M], ALU.add)\
                    .then_inc(folds, 1)

            def batch_tile(bt, take=True, late=True, last=False):
                for q in range(QG):
                    for j in range(JT):
                        i = JT * q + j
                        if j == 1 and not (last and q == QG - 1):
                            spread(bt if q < QG - 1 else bt + 1, (q + 1) % QG)
                        if take and i == GATHER_FROM - 1:
                            pool.wait_ge(gathered, 16 * NF * (bt + 2))
                        if take and i == GATHER_FROM:
                            pool.wait_ge(ids_ready, bt + 3)
                            pool.wait_ge(rows_split, bt + 2)
                        fold(bt, q, j)
                        if take and i == GATHER_FROM - 1:
                            take_ids(bt + 2)
                        if take and i >= GATHER_FROM:
                            gather(range(GATHERS * (i - GATHER_FROM), GATHERS * (i - GATHER_FROM + 1)))
                        if late and i * GATHERS + EARLY < NF:
                            gather(range(EARLY + GATHERS * i, min(EARLY + GATHERS * (i + 1), NF)))

            pool.wait_ge(ids_in, 16)
            take_ids(0)
            pool.wait_ge(ids_ready, 1)
            gather(range(NF))
            pool.wait_ge(gathered, 16 * NF)
            take_ids(1)
            pool.wait_ge(ids_ready, 2)
            pool.wait_ge(rows_split, 1)
            gather(range(EARLY))
            pool.wait_ge(consts_made, 7)
            pool.wait_ge(ones_set, 1)
            pool.wait_ge(block_ready, 2)
            spread(0, 0)
            batch_tile(0)
            with pool.Fori(1, BT - 2) as bt:
                batch_tile(bt)
            batch_tile(BT - 2, take=False)
            batch_tile(BT - 1, take=False, late=False, last=True)

        @blk.scalar
        def _(act):
            load_f0(act, pieces[1::2])
            lo = 0
            for i, hi in enumerate(f1_cuts):
                act.wait_ge(f1_in[i], 16)
                act.activation(f1_high[:, lo:hi, :].rearrange("p f m -> p (f m)"), f1_raw[:, lo * M:hi * M],
                               ACT.Copy).then_inc(f1_high_ready, 1)
                lo = hi
            for h in range(2):
                act.wait_ge(dense_filled, h + 1)
                act.activation(z_dense[:, h * 512:(h + 1) * 512], Y[h][0:D, :], ACT.Copy).then_inc(dense_read, 1)

            def split_rows(bt):
                act.wait_ge(gathered, 16 * NF * (bt + 1))
                if not (isinstance(bt, int) and bt == 0):
                    act.wait_ge(x_filled, FILLS * (bt - 1) + QG)
                act.activation(rows_parts[:, :, 0, :], rows[:].rearrange("p (f d) -> p d f", d=D),
                               ACT.Copy).then_inc(rows_high_ready, 1)

            def read_transposes(bt, g):
                act.wait_ge(x_filled, FILLS * bt + g + 1)
                act.activation(x_parts[:, :, 4 * g:4 * g + 4],
                               X[g % 2][0:2 * NF, :].rearrange("p (d b) -> p b d", d=4),
                               ACT.Copy).then_inc(x_read, 1)

            def read_fields(bt, q):
                n = QG + FILLS_G * q
                act.wait_ge(x_filled, FILLS * bt + n + 1)
                if not (isinstance(bt, int) and QG * bt + q == 0):
                    act.wait_ge(pairs_ready, DVE_READS * bt + K0 * q)
                act.activation(fields[:], X[n % 2][0:SEL, :], ACT.Copy).then_inc(x_read, 1)

            def read_scalars(bt, q):
                n = QG + FILLS_G * q + 1
                act.wait_ge(x_filled, FILLS * bt + n + 1)
                if isinstance(bt, int) and bt == 0 and q < 2:
                    act.wait_ge(ones_set, 1)
                act.activation(x_col[:, q % 2, :, 0:NF],
                               X[n % 2][:, 0:JT * FC].rearrange("p (j f) -> p j f", f=FC)[:, :, 0:NF],
                               ACT.Copy).then_inc(x_read, 1)

            def split_cur0(bt, q):
                act.wait_ge(cur0_summed, K0 * (QG * bt + q + 1))
                act.activation(cur0_high[:, q % 2, :], C[:], ACT.Copy).then_inc(cur0_high_ready, 1)

            def read_g(bt, q, j):
                t = column_tile(bt, q, j)
                act.wait_ge(g_filled, t + 1)
                half = G[:, bass.ds((bt % 2) * (FC * P), FC * P)].rearrange("p (f b) -> p f b", b=P)
                b0 = GB * q + TB * j
                act.activation(half[:, :, b0:b0 + TB], GP[:, 0:TB * FC].rearrange("p (b f) -> p f b", b=TB),
                               ACT.Copy).then_inc(g_read, 1)

            def scale_chunk(bt, q, j, c):
                t = column_tile(bt, q, j)
                n = SCALED.index(c)
                act.wait_ge(y_filled, CH * t + c + 1)
                if n == 0:
                    if not (isinstance(t, int) and t < 2):
                        act.wait_ge(folds, 3 * (t - 1))
                    dst = acc_s[:, j % 2, :]
                else:
                    back = n - PR
                    if back >= 1:
                        act.wait_ge(acc_steps, NST * t + STEP_DONE[SCALED[back]])
                    elif not (isinstance(t, int) and t == 0):
                        act.wait_ge(acc_steps, NST * (t - 1) + STEP_DONE[SCALED[back + NSC - 1]])
                    dst = scaled_sb[:, (n - 1) % PR, :]
                for i, f in enumerate(CH_F[c]):
                    ins = act.activation(dst[:, i * M:(i + 1) * M],
                                         Y[(SLOTS * q + CH * j + c) % YB][:, i * M:(i + 1) * M],
                                         ACT.Copy, scale=x_col[:, q % 2, j, f:f + 1])
                ins.then_inc(scaled, 1)

            def group(bt, q, first=False, last=False):
                nbt, nq = (bt, q + 1) if q < QG - 1 else (bt + 1, 0)
                for s in range(SLOTS):
                    j, c = divmod(s, CH)
                    if not last:
                        if nq == 0 and s < QG:
                            read_transposes(nbt, s)
                        if s == AT_FIELDS:
                            read_fields(nbt, nq)
                        if s == AT_SCALARS:
                            read_scalars(nbt, nq)
                        if s == AT_SPLIT:
                            split_cur0(nbt, nq)
                        if q == 2 and s == 20 and not (isinstance(bt, int) and bt == BT - 1):
                            split_rows(bt + 1)
                    if c == AT_GREAD and not (first and j == 0):
                        pj = (j - 1) % JT
                        pq = q if j else (q - 1) % QG
                        read_g(bt if j or q else bt - 1, pq, pj)
                    if c in SCALED:
                        scale_chunk(bt, q, j, c)

            split_rows(0)
            for g in range(QG):
                read_transposes(0, g)
            read_fields(0, 0)
            read_scalars(0, 0)
            split_cur0(0, 0)
            for q in range(QG):
                group(0, q, first=q == 0)
            with act.Fori(1, BT - 1) as bt:
                for q in range(QG):
                    group(bt, q)
            for q in range(QG):
                group(BT - 1, q, last=q == QG - 1)
            read_g(BT - 1, QG - 1, JT - 1)

            act.wait_ge(mlp_in, 96)
            for h in range(2):
                for m in range(4):
                    act.wait_ge(m1_filled, 4 * h + m + 1)
                    act.activation(h1[:, m, h * 512:(h + 1) * 512], Y[m][:], ACT.Relu,
                                   bias=b1_sb[:, m:m + 1]).then_inc(m1_read, 1)
                for m in range(2):
                    act.wait_ge(m2_filled, 2 * h + m + 1)
                    if h:
                        act.wait_ge(m3_filled, 1)
                    act.activation(h2[:, m, :], X[m][:], ACT.Relu, bias=b2_sb[:, m:m + 1]).then_inc(m2_read, 1)
                act.wait_ge(m3_filled, h + 1)
                act.activation(y[:, h * 512:(h + 1) * 512], C[0:1, :], ACT.Copy).then_inc(m3_read, 1)

        @blk.vector
        def _(dve):
            dve.memset(f0_mirror[0:NF, 0, :], 0.0).then_inc(mirror_zero, 1)
            dve.memset(x_col[:, :, :, NF:FC], 1.0).then_inc(ones_set, 1)
            dve.wait_ge(consts_made, 7)
            dve.tensor_copy(ident_r[:], ident[:]).then_inc(sel_ready, 1)
            dve.tensor_copy(comb_r[:], comb[:, 0:FC]).then_inc(sel_ready, 1)
            for i in range(1 + K0):
                for s in range(SPK):
                    off = 0 if i == 0 else min(SPK * (i - 1) + s, SHIFTS)
                    ins = dve.tensor_copy(select[:, i, s * NF:(s + 1) * NF], comb[:, off % NF:off % NF + NF])
                    ins.then_inc(sel_ready, 1)
            dve.wait_ge(f0_in, 16 * len(pieces))
            dve.wait_ge(mirror_zero, 1)
            n = K0 - 1
            dve.tensor_tensor(f0_sum[:, 0:n, :], f0_sum[:, 0:n, :], f0_mirror[:, 0:n, :], ALU.add).then_inc(f0_ready, 1)
            r = K0_ROWS[n]
            dve.tensor_tensor(f0_sum[0:r, n, :], f0_sum[0:r, n, :], f0_mirror[0:r, n, :], ALU.add).then_inc(f0_ready, 1)
            lo = 0
            for i, hi in enumerate(f1_cuts):
                dve.wait_ge(f1_high_ready, i + 1)
                dve.tensor_tensor(f1_low[:, lo:hi, :].rearrange("p f m -> p (f m)"), f1_raw[:, lo * M:hi * M],
                                  f1_high[:, lo:hi, :].rearrange("p f m -> p (f m)").bitcast(F32),
                                  ALU.subtract).then_inc(f1_ready, 1)
                lo = hi

            def split_rows(bt):
                dve.wait_ge(rows_high_ready, bt + 1)
                dve.tensor_tensor(rows_parts[:, :, 1, :], rows[:].rearrange("p (f d) -> p d f", d=D),
                                  rows_parts[:, :, 0, :].bitcast(F32), ALU.subtract).then_inc(rows_split, 1)

            def pair(bt, q, k):
                n = QG + FILLS_G * q + 2 + k
                z = DVE_READS * bt + K0 * q + k
                dve.wait_ge(x_filled, FILLS * bt + n + 1)
                if k == 0:
                    dve.wait_ge(x_read, ACT_READS * bt + fill_reader(QG + FILLS_G * q)[1])
                if not (isinstance(z, int) and z < 2):
                    dve.wait_ge(cur0_summed, z - 1)
                r = K0_ROWS[k]
                dve.tensor_tensor(pairs[0:r, (K0 * q + k) % 2, :], X[n % 2][0:r, :], fields[0:r, :],
                                  ALU.mult).then_inc(pairs_ready, 1)

            def split_cur0(bt, q):
                g = QG * bt + q
                dve.wait_ge(cur0_high_ready, g + 1)
                dve.tensor_tensor(cur0_low[:, q % 2, :], C[:], cur0_high[:, q % 2, :].bitcast(F32),
                                  ALU.subtract).then_inc(cur0_ready, 1)
                dve.tensor_reduce(z0[:, bass.ds(P * bt + GB * q, GB)],
                                  C[:].rearrange("p (b d) -> p b d", d=D), AX.X, ALU.add).then_inc(cur0_read, 1)

            def layer2_read(bt, part):
                n = L2_PARTS * bt + part
                dve.wait_ge(l2_filled, n + 1)
                z = z2[:, bass.ds(P * bt, P)]
                if part == 0:
                    dve.tensor_copy(z, C[:, 0:P]).then_inc(l2_read, 1)
                else:
                    dve.wait_ge(l2_read, n)
                    dve.tensor_tensor(z, C[:, 0:P], z, ALU.add).then_inc(l2_read, 1)

            def copy_z1(bt):
                dve.wait_ge(g_read, TPB * (bt + 1))
                dve.tensor_copy(z1[:, bass.ds(P * bt, P)], G[:, bass.ds((bt % 2) * (FC * P) + NF * P, P)])\
                    .then_inc(z1_copied, 1)

            def step(bt, q, j, n):
                kind, c, i = STEPS[n]
                t = column_tile(bt, q, j)
                xs = x_col[:, q % 2, j, :]
                if kind == "add":
                    if n == STEPS.index(("add", SCALED[1], 0)):
                        pass
                    else:
                        before = max(m for m in range(n) if STEPS[m][0] == "add")
                        dve.wait_ge(acc_steps, NST * t + before + 1)
                    dve.wait_ge(scaled, NSC * t + SCALED.index(c) + 1)
                    w = M * len(CH_F[c])
                    a = acc_s[:, j % 2, 0:w]
                    dve.tensor_tensor(a, a, scaled_sb[:, (SCALED.index(c) - 1) % PR, 0:w], ALU.add)\
                        .then_inc(acc_steps, 1)
                    return
                fused = [m for m in range(n) if STEPS[m][0] == "fuse"]
                f = CH_F[c][i]
                src = Y[(SLOTS * q + CH * j + c) % YB][:, i * M:(i + 1) * M]
                half = acc_f[:, j % 2, (len(fused) % 2) * M:(len(fused) % 2 + 1) * M]
                if i == 0:
                    dve.wait_ge(y_filled, CH * t + c + 1)
                if not fused and not (isinstance(t, int) and t < 2):
                    dve.wait_ge(folds, 3 * (t - 1))
                if len(fused) < 2:
                    dve.tensor_scalar(half, src, xs[:, f:f + 1], None, ALU.mult).then_inc(acc_steps, 1)
                else:
                    dve.wait_ge(acc_steps, NST * t + fused[-2] + 1)
                    dve.scalar_tensor_tensor(half, src, xs[:, f:f + 1], half, ALU.mult, ALU.add)\
                        .then_inc(acc_steps, 1)

            def group(bt, q, layer2=True, last=False):
                nbt, nq = (bt, q + 1) if q < QG - 1 else (bt + 1, 0)
                for s in range(SLOTS):
                    j, c = divmod(s, CH)
                    if layer2 and q and s == 5:
                        layer2_read(bt - 1, q - 1)
                    if layer2 and q == 1 and s == 7:
                        copy_z1(bt - 1)
                    if not last:
                        if s in AT_PAIR:
                            pair(nbt, nq, AT_PAIR.index(s))
                        if s == AT_SPLIT:
                            split_cur0(nbt, nq)
                        if q == 2 and s == 20 and not (isinstance(bt, int) and bt == BT - 1):
                            split_rows(bt + 1)
                    now = [n for n in range(NST) if STEPS[n][0] == "fuse" and STEPS[n][1] == c
                           or STEPS[n][0] == "add" and STEPS[n][1] == c - 1]
                    for n in now:
                        step(bt, q, j, n)

            split_rows(0)
            for k in range(K0):
                pair(0, 0, k)
            split_cur0(0, 0)
            for q in range(QG):
                group(0, q, layer2=False)
            with dve.Fori(1, BT - 1) as bt:
                for q in range(QG):
                    group(bt, q)
            for q in range(QG):
                group(BT - 1, q, last=q == QG - 1)
            copy_z1(BT - 1)
            for part in range(L2_PARTS):
                layer2_read(BT - 1, part)

        @blk.tensor
        def _(pe):
            pe.wait_ge(consts_made, 7)
            pe.wait_ge(dense_in, 16)
            for t in range(BT):
                ins = pe.matmul(Y[t // 4][0:D, (t % 4) * P:(t % 4 + 1) * P], dense_sb[:, t, :], ident[:],
                                start=True, stop=True)
                if t % 4 == 3:
                    ins.then_inc(dense_filled, 1)

            def x_free(bt, n):
                if isinstance(bt, int) and bt == 0 and n < 2:
                    return
                before, m = (bt, n - 2) if n >= 2 else (bt - 1, n - 2 + FILLS)
                by_vector, count = fill_reader(m)
                if by_vector:
                    pe.wait_ge(pairs_ready, DVE_READS * before + count)
                else:
                    pe.wait_ge(x_read, ACT_READS * before + count)

            def transposes(bt, g):
                x_free(bt, g)
                pe.wait_ge(rows_split, bt + 1)
                for i in range(4):
                    ins = pe.matmul(X[g % 2][0:2 * NF, i * P:(i + 1) * P],
                                    rows_parts[:, 4 * g + i, :, :].rearrange("p h f -> p (h f)"), ident_r[:],
                                    start=True, stop=True)
                ins.then_inc(x_filled, 1)

            x_cols = x_parts[:].rearrange("p b d -> p (b d)")

            def selection(bt, q, i):
                n = QG + FILLS_G * q + (0 if i == 0 else 1 + i)
                x_free(bt, n)
                if i == 0:
                    pe.wait_ge(x_read, ACT_READS * bt + QG)
                r = SEL if i == 0 else K0_ROWS[i - 1]
                pe.matmul(X[n % 2][0:r, :], select[:, i, 0:r], x_cols[:, q * GN:(q + 1) * GN],
                          start=True, stop=True).then_inc(x_filled, 1)

            def scalars(bt, q):
                n = QG + FILLS_G * q + 1
                x_free(bt, n)
                for j in range(JT):
                    ins = pe.matmul(X[n % 2][:, j * FC:(j + 1) * FC],
                                    x_cols[:, q * GN + j * P:q * GN + (j + 1) * P], comb_r[:],
                                    start=True, stop=True)
                ins.then_inc(x_filled, 1)

            def cur0_sum(bt, q, k, after_layer2):
                z = DVE_READS * bt + K0 * q + k
                pe.wait_ge(pairs_ready, z + 1)
                if k == 0:
                    if after_layer2 is not None:
                        pe.wait_ge(l2_read, after_layer2)
                    elif not (isinstance(bt, int) and QG * bt + q == 0):
                        pe.wait_ge(cur0_read, QG * bt + q)
                r = K0_ROWS[k]
                pe.matmul(C[:], f0_sum[0:r, k, :], pairs[0:r, (K0 * q + k) % 2, :],
                          start=k == 0, stop=k == K0 - 1).then_inc(cur0_summed, 1)

            def g_product(bt, q, j):
                t = column_tile(bt, q, j)
                pe.wait_ge(folds, 3 * (t + 1))
                pe.wait_ge(block_made, QG * bt + q + 1)
                if not (isinstance(t, int) and t == 0):
                    pe.wait_ge(g_read, t)
                pe.matmul(GP[:, 0:TB * FC], cur1[:, j % 2, :], x_block[:, q % 2, j, :],
                          start=True, stop=True).then_inc(g_filled, 1)

            def layer2(bt, part, fs):
                first, end = L2_F * part, L2_F * (part + 1)
                if fs[0] == first:
                    pe.wait_ge(g_read, TPB * (bt + 1))
                    pe.wait_ge(cur0_read, min(QG * (bt + 1) + part + 2, QG * BT) if isinstance(bt, int)
                               else QG * (bt + 1) + part + 2)
                    if bt is BT - 1 and part:
                        pe.wait_ge(l2_read, L2_PARTS * bt + part)
                for f in fs:
                    ins = pe.matmul(C[:, 0:P], f2_sb[:, f, :], G[:, bass.ds((bt % 2) * (FC * P) + f * P, P)],
                                    start=f == first, stop=f == end - 1)
                if fs[-1] == end - 1:
                    ins.then_inc(l2_filled, 1)

            def chunk(bt, q, j, c):
                t = column_tile(bt, q, j)
                if not (isinstance(t, int) and t == 0 and c < YB):
                    before, pc = (t, c - YB) if c >= YB else (t - 1, c - YB + CH)
                    if pc in FUSED:
                        pe.wait_ge(acc_steps, NST * before + STEP_DONE[pc])
                    else:
                        pe.wait_ge(scaled, NSC * before + SCALED.index(pc) + 1)
                bank = Y[(SLOTS * q + CH * j + c) % YB][:, 0:M * len(CH_F[c])]
                lo, hi = CH_F[c][0], CH_F[c][-1] + 1
                wh = f1_high[:, lo:hi, :].rearrange("p f m -> p (f m)")
                wl = f1_low[:, lo:hi, :].rearrange("p f m -> p (f m)")
                ch = cur0_high[:, q % 2, j * P:(j + 1) * P]
                cl = cur0_low[:, q % 2, j * P:(j + 1) * P]
                pe.matmul(bank, ch, wh, start=True, stop=False)
                pe.matmul(bank, ch, wl, start=False, stop=False)
                pe.matmul(bank, cl, wh, start=False, stop=True).then_inc(y_filled, 1)

            l2_slices = [range(0, 4), range(4, 7), range(7, 10), range(10, 13)]

            def group(bt, q, with_layer2=True, first=False, last=False):
                nbt, nq = (bt, q + 1) if q < QG - 1 else (bt + 1, 0)
                for s in range(SLOTS):
                    j, c = divmod(s, CH)
                    if s == 0:
                        pe.wait_ge(cur0_ready, QG * bt + q + 1)
                    if not last:
                        if nq == 0 and s < QG:
                            transposes(nbt, s)
                        if s == AT_FIELDS:
                            selection(nbt, nq, 0)
                        if s == AT_SCALARS:
                            scalars(nbt, nq)
                        if s in AT_PAIR:
                            selection(nbt, nq, 1 + AT_PAIR.index(s))
                        if s in AT_SUM:
                            after = L2_PARTS * (bt - 1) + q if with_layer2 and q else None
                            cur0_sum(nbt, nq, AT_SUM.index(s), after)
                    if with_layer2 and q and s < 4:
                        layer2(bt - 1, q - 1, [L2_F * (q - 1) + f for f in l2_slices[s]])
                    if c == AT_G and not (first and j == 0):
                        pj = (j - 1) % JT
                        pq = q if j else (q - 1) % QG
                        g_product(bt if j or q else bt - 1, pq, pj)
                    chunk(bt, q, j, c)

            pe.wait_ge(sel_ready, 2 + SPK * (1 + K0))
            for g in range(QG):
                transposes(0, g)
            selection(0, 0, 0)
            scalars(0, 0)
            pe.wait_ge(f0_ready, 2)
            for k in range(K0):
                selection(0, 0, 1 + k)
                cur0_sum(0, 0, k, None)
            pe.wait_ge(f1_ready, len(f1_cuts))
            pe.wait_ge(dense_read, 2)
            pe.wait_ge(f2_in, 16)
            for q in range(QG):
                group(0, q, with_layer2=False, first=q == 0)
            with pe.Fori(1, BT - 1) as bt:
                for q in range(QG):
                    group(bt, q)
            for q in range(QG):
                group(BT - 1, q, last=q == QG - 1)
            g_product(BT - 1, QG - 1, JT - 1)
            for part in range(L2_PARTS):
                layer2(BT - 1, part, [L2_F * part + f for f in range(L2_F)])

            pe.wait_ge(mlp_in, 96)
            pe.wait_ge(z1_copied, BT)
            pe.wait_ge(l2_read, L2_PARTS * BT)
            pe.wait_ge(acc_steps, NST * TPB * BT)
            pe.wait_ge(scaled, NSC * TPB * BT)
            for h in range(2):
                cols = slice(h * 512, (h + 1) * 512)
                for m in range(4):
                    if h:
                        pe.wait_ge(m1_read, m + 1)
                    for k, z in enumerate((z0, z1, z2)):
                        pe.matmul(Y[m][:], w1_sb[:, k, m * P:(m + 1) * P], z[:, cols], start=k == 0, stop=False)
                    pe.matmul(Y[m][:], w1_dense[:, m * P:(m + 1) * P], z_dense[:, cols], start=False, stop=True)\
                        .then_inc(m1_filled, 1)
                for m in range(2):
                    if h:
                        pe.wait_ge(m2_read, m + 1)
                    for k in range(4):
                        if m == 0:
                            pe.wait_ge(m1_read, 4 * h + k + 1)
                        ins = pe.matmul(X[m][:], w2_sb[:, k, m * P:(m + 1) * P], h1[:, k, cols],
                                        start=k == 0, stop=k == 3)
                    ins.then_inc(m2_filled, 1)
                if h:
                    pe.wait_ge(m3_read, 1)
                for k in range(2):
                    pe.wait_ge(m2_read, 2 * h + k + 1)
                    ins = pe.matmul(C[0:1, :], w3_sb[:, k:k + 1], h2[:, k, :], start=k == 0, stop=k == 1)
                ins.then_inc(m3_filled, 1)


_INS = (["dense_ctx", "ids"] + [f"tbl_{i}" for i in range(39)]
        + ["W_top1", "b_top1", "W_top2", "b_top2", "W_top3", "L0_rec_f0", "L0_rec_f1", "L0_rec_f2"])


def kernel(**inputs):
    import numpy as _np
    import concourse.bacc as _bacc
    from concourse import mybir as _mybir
    from concourse.bass_utils import run_bass_kernel_spmd as _run

    nc = _bacc.Bacc("TRN2", target_bir_lowering=False, num_devices=1)
    arrays, args = {}, {}
    for name in _INS:
        a = _np.ascontiguousarray(inputs[name])
        arrays[f"in_{name}_dram"] = a
        args[name] = nc.dram_tensor(f"in_{name}_dram", a.shape, _mybir.dt.from_np(a.dtype), kind="ExternalInput").ap()
    out = nc.dram_tensor("out_0_dram", (B, 1), _mybir.dt.float32, kind="ExternalOutput").ap()
    build(nc, args["dense_ctx"], args["ids"], [args[f"tbl_{i}"] for i in range(39)],
          args["W_top1"], args["b_top1"], args["W_top2"], args["b_top2"], args["W_top3"],
          args["L0_rec_f0"], args["L0_rec_f1"], args["L0_rec_f2"], out)
    r = _run(nc, [arrays], core_ids=[0])
    return r.results[0]["out_0_dram"]
```

```python
from contextlib import ExitStack

import concourse.bass as bass
from concourse import mybir

F32 = mybir.dt.float32
F32R = mybir.dt.float32r
I32 = mybir.dt.int32
ALU = mybir.AluOpType
ACT = mybir.ActivationFunctionType
AX = mybir.AxisListType

P = 128
B, NF, D = 1024, 39, 16
M = 128
BT = B // P
QG = 4
GB = P // QG
GN = GB * D
JT = GN // P
TB = P // D
TPB = QG * JT
FC = NF + 1

SHIFTS = NF // 2 + 1
BLK = P // NF
K0 = -(-SHIFTS // BLK)
K0_ROWS = [NF * sum(k + K0 * j < SHIFTS for j in range(BLK)) for k in range(K0)]
SEL = BLK * NF
SEQ = SEL + K0 - 1

CH = -(-NF // 4)
CH_F = [range(4 * c, min(4 * c + 4, NF)) for c in range(CH)]
FUSED = (3, 6, 9)
SCALED = tuple(c for c in range(CH) if c not in FUSED)
YB = 4
PR = 3
SLOTS = JT * CH

AT_ROWS = 35
AT_SCALARS = 5
AT_PAIR = [6 + 4 * k for k in range(K0)]
AT_SUM = [10 + 4 * k for k in range(K0)]
AT_SPLIT = 35
AT_G, AT_GREAD = 7, 8
L2_PARTS = 3
L2_F = NF // L2_PARTS
GATHERS = 3
GATHER_FROM = 9
EARLY = GATHERS * (TPB - GATHER_FROM)


def vector_steps():
    steps, held = [], None
    for c in range(CH):
        if c in FUSED:
            steps += [("fuse", c, i) for i in range(len(CH_F[c]))]
        if held is not None:
            steps.append(("add", held, 0))
            held = None
        if c in SCALED[1:]:
            held = c
    return steps


STEPS = vector_steps()
NST = len(STEPS)
STEP_DONE = {c: max(n for n, s in enumerate(STEPS) if s[1] == c) + 1 for _, c, _ in STEPS}
NSC = len(SCALED)

FILLS = QG + QG
COPIES = BLK + K0


def build(nc, dense, ids, tables, w1, b1, w2, b2, w3, f0, f1, f2, out):
    ctx = ExitStack()
    with ctx:
        def sb(name, shape, dt=F32):
            return ctx.enter_context(nc.sbuf_tensor(name, shape, dt))

        def ps(name):
            return ctx.enter_context(nc.psum_tensor(name, [P, 512], F32))

        def sem(name):
            return ctx.enter_context(nc.semaphore(name))

        f1_high = sb("f1_high", [P, NF, M], F32R)
        f1_low = sb("f1_low", [P, NF, M], F32R)
        f2_sb = sb("f2_sb", [P, NF, M])
        f0_sum = sb("f0_sum", [SEL, K0, M])
        b1_sb = sb("b1_sb", [P, 4])
        b2_sb = sb("b2_sb", [P, 2])
        ident = sb("ident", [P, P])
        block = sb("block", [P, TB])
        ids_sb = sb("ids_sb", [P, BT, NF], I32)
        ids_now = sb("ids_now", [P, NF], I32)
        rows = sb("rows", [P, NF * D])
        rows_seq = sb("rows_seq", [P, D, SEQ])
        x_seq = sb("x_seq", [SEQ, P, D])
        shifted = sb("shifted", [P, 2, 1 + K0, GN])
        pairs = sb("pairs", [SEL, 2, GN])
        cur0_high = sb("cur0_high", [P, 2, GN], F32R)
        cur0_low = sb("cur0_low", [P, 2, GN], F32R)
        x_col = sb("x_col", [P, QG, JT, FC])
        scaled_sb = sb("scaled_sb", [P, PR, 4 * M])
        acc_s = sb("acc_s", [P, 2, 4 * M])
        acc_f = sb("acc_f", [P, 2, 2 * M])
        cur1 = sb("cur1", [P, 2, M])
        x_block = sb("x_block", [P, 2, JT, TB * FC])
        G = sb("G", [P, 2 * FC * P])
        f1_raw = G[:, 0:NF * M]
        f0_mirror = G[0:SEL, FC * P:FC * P + K0 * M].rearrange("p (k m) -> p k m", m=M)
        dense_sb = G[:, FC * P + K0 * M:FC * P + K0 * M + BT * D].rearrange("p (t c) -> p t c", t=BT)
        h1 = G[:, 0:4 * B].rearrange("p (m b) -> p m b", m=4)
        h2 = G[:, 4 * B:4 * B + 2 * 512].rearrange("p (m b) -> p m b", m=2)
        late = shifted[:].rearrange("p a k n -> p (a k n)")
        w1_sb = late[:, 0:3 * 512].rearrange("p (k n) -> p k n", k=3)
        w1_dense = late[0:D, 3 * 512:4 * 512]
        w2_sb = late[:, 4 * 512:6 * 512].rearrange("p (k n) -> p k n", k=4)
        w3_sb = late[:, 6 * 512:6 * 512 + 2]
        y = late[0:1, 7 * 512:9 * 512]
        z0, z1, z2 = sb("z0", [P, B]), sb("z1", [P, B]), sb("z2", [P, B])
        z_dense = sb("z_dense", [D, B])

        Y = [ps(f"Y{i}") for i in range(YB)]
        X = [ps("X0"), ps("X1")]
        C = ps("C")
        GP = ps("GP")

        ids_in, ids_ready, gathered = sem("ids_in"), sem("ids_ready"), sem("gathered")
        consts_made, block_ready = sem("consts_made"), sem("block_ready")
        mirror_zero, f0_in, f0_ready = sem("mirror_zero"), sem("f0_in"), sem("f0_ready")
        f1_in, f1_high_ready, f1_ready = [sem(f"f1_in{i}") for i in range(3)], sem("f1_high_ready"), sem("f1_ready")
        f2_in, dense_in, mlp_in = sem("f2_in"), sem("dense_in"), sem("mlp_in")
        dense_filled, dense_read = sem("dense_filled"), sem("dense_read")
        rows_taken, copied = sem("rows_taken"), [sem("copied_even"), sem("copied_odd")]
        x_filled, x_read, pairs_ready = sem("x_filled"), sem("x_read"), sem("pairs_ready")
        cur0_summed, cur0_high_ready, cur0_ready, cur0_read = (
            sem("cur0_summed"), sem("cur0_high_ready"), sem("cur0_ready"), sem("cur0_read"))
        y_filled, scaled, acc_steps, folds = sem("y_filled"), sem("scaled"), sem("acc_steps"), sem("folds")
        ones_set, block_made = sem("ones_set"), sem("block_made")
        g_filled, g_read = sem("g_filled"), sem("g_read")
        l2_filled, l2_read, z1_copied = sem("l2_filled"), sem("l2_read"), sem("z1_copied")
        m1_filled, m1_read, m2_filled, m2_read, m3_filled, m3_read = (
            sem("m1_filled"), sem("m1_read"), sem("m2_filled"), sem("m2_read"), sem("m3_filled"), sem("m3_read"))
        y_out = sem("y_out")

        f1_cuts = [13, 26, 39]

        def f0_pieces():
            for k in range(K0):
                for p0 in range(0, K0_ROWS[k], NF):
                    a = [(f - K0 * (p0 // NF)) % NF for f in range(NF)]
                    b = [(f + k) % NF for f in range(NF)]
                    for mirror in (False, True)[:1 + (b != a)]:
                        src = [NF * v + u if mirror else NF * u + v for u, v in zip(a, b)]
                        cuts = [0] + [f for f in range(1, NF) if src[f] - src[f - 1] != NF + 1] + [NF]
                        for lo, hi in zip(cuts, cuts[1:]):
                            yield mirror, k, p0 + lo, hi - lo, src[lo], NF + 1

        pieces = list(f0_pieces())

        def load_f0(eng):
            for mirror, k, p0, n, first, step in pieces:
                dst = (f0_mirror if mirror else f0_sum)[p0:p0 + n, k, :]
                eng.dma_start(dst, f0[first:first + step * (n - 1) + 1:step, :]).then_inc(f0_in, 16)

        def column_tile(bt, q, j):
            return TPB * bt + JT * q + j

        blk = ctx.enter_context(nc.Block())

        @blk.sync
        def _(sp):
            sp.dma_start(ids_sb[:], ids.rearrange("(t p) f -> p t f", p=P)).then_inc(ids_in, 16)
            lo = 0
            for i, hi in enumerate(f1_cuts):
                sp.dma_start(f1_raw[:, lo * M:hi * M].rearrange("p (f m) -> p f m", m=M),
                             f1.rearrange("(f g) m -> g f m", g=M)[:, lo:hi, :]).then_inc(f1_in[i], 16)
                lo = hi
            sp.dma_start(dense_sb, dense.rearrange("(t p) c -> p t c", p=P)).then_inc(dense_in, 16)
            load_f0(sp)
            sp.dma_start(f2_sb[:], f2.rearrange("(f g) m -> g f m", g=M)).then_inc(f2_in, 16)
            sp.dma_start(b1_sb[:], b1.rearrange("(m p) -> p m", p=P),
                         allow_slow_non_contiguous=True).then_inc(mlp_in, 16)
            sp.dma_start(b2_sb[:], b2.rearrange("(m p) -> p m", p=P),
                         allow_slow_non_contiguous=True).then_inc(mlp_in, 16)

            def shift_copies(bt, q):
                group = QG * bt + q
                if q == 0:
                    sp.wait_ge(x_read, FILLS * bt + QG)
                if not (isinstance(group, int) and group < 2):
                    sp.wait_ge(pairs_ready, K0 * (group - 1))
                cols = x_seq[:].rearrange("p b d -> p (b d)")[:, GN * q:GN * (q + 1)]
                for j in range(BLK):
                    off = -K0 * j % NF
                    sp.dma_start(shifted[j * NF:(j + 1) * NF, q % 2, 0, :], cols[off:off + NF, :])\
                      .then_inc(copied[q % 2], 16)
                for k in range(K0):
                    r = K0_ROWS[k]
                    sp.dma_start(shifted[0:r, q % 2, 1 + k, :], cols[k:k + r, :]).then_inc(copied[q % 2], 16)

            for q in range(QG):
                shift_copies(0, q)
            with sp.Fori(1, BT) as bt:
                for q in range(QG):
                    shift_copies(bt, q)
            sp.wait_ge(pairs_ready, K0 * QG * BT)
            sp.dma_start(w1_sb, w1[0:3 * P, :].rearrange("(k p) n -> p k n", p=P)).then_inc(mlp_in, 16)
            sp.dma_start(w1_dense, w1[3 * P:3 * P + D, :]).then_inc(mlp_in, 16)
            sp.dma_start(w2_sb, w2.rearrange("(k p) n -> p k n", p=P)).then_inc(mlp_in, 16)
            sp.dma_start(w3_sb, w3.rearrange("(k p) o -> p (k o)", p=P),
                         allow_slow_non_contiguous=True).then_inc(mlp_in, 16)
            sp.wait_ge(m3_read, 2)
            sp.dma_start(out.rearrange("b o -> o b"), y).then_inc(y_out, 16)
            sp.wait_ge(y_out, 16)

        @blk.gpsimd
        def _(pool):
            pool.memset(ident[:], 0.0).then_inc(consts_made, 1)
            pool.memset(block[:], 1.0).then_inc(consts_made, 1)
            pool.wait_ge(consts_made, 2)
            pool.affine_select(out=ident[:], in_=ident[:], compare_op=ALU.not_equal, fill=1.0, base=0,
                               pattern=[[-1, P]], channel_multiplier=1).then_inc(consts_made, 1)
            pool.affine_select(out=block[:], in_=block[:], compare_op=ALU.is_ge, fill=0.0, base=0,
                               pattern=[[-D, TB]], channel_multiplier=1).then_inc(block_ready, 1)
            pool.wait_ge(block_ready, 1)
            pool.affine_select(out=block[:], in_=block[:], compare_op=ALU.is_ge, fill=0.0, base=D - 1,
                               pattern=[[D, TB]], channel_multiplier=-1).then_inc(block_ready, 1)

            def take_ids(bt):
                pool.tensor_copy(ids_now[:], ids_sb[:, bass.ds(bt, 1), :].rearrange("p o f -> p (o f)"))\
                    .then_inc(ids_ready, 1)

            def gather(fs):
                for f in fs:
                    pool.indirect_dma_start(
                        out=rows[:, f * D:(f + 1) * D], out_offset=None, in_=tables[f],
                        in_offset=bass.IndirectOffsetOnAxis(ap=ids_now[:, f:f + 1], axis=0),
                    ).then_inc(gathered, 16)

            def spread(bt, q):
                group = QG * bt + q
                pool.wait_ge(x_read, FILLS * bt + QG + q + 1)
                if not (isinstance(bt, int) and QG * bt + q < 2):
                    pool.wait_ge(g_filled, JT * (group - 1))
                for j in range(JT):
                    ins = pool.tensor_tensor(
                        x_block[:, q % 2, j, :].rearrange("p (b f) -> p b f", b=TB),
                        x_col[:, q, j, :].unsqueeze(1).broadcast_to([P, TB, FC]),
                        block[:].unsqueeze(2).broadcast_to([P, TB, FC]), ALU.mult)
                ins.then_inc(block_made, 1)

            def fold(bt, q, j):
                t = column_tile(bt, q, j)
                pool.wait_ge(acc_steps, NST * (t + 1))
                a, f = acc_s[:, j % 2, :], acc_f[:, j % 2, :]
                pool.tensor_tensor(a[:, 0:2 * M], a[:, 0:2 * M], a[:, 2 * M:4 * M], ALU.add).then_inc(folds, 1)
                pool.wait_ge(folds, 3 * t + 1)
                pool.tensor_tensor(f, f, a[:, 0:2 * M], ALU.add).then_inc(folds, 1)
                pool.wait_ge(folds, 3 * t + 2)
                if not (isinstance(t, int) and t < 2):
                    pool.wait_ge(g_filled, t - 1)
                pool.tensor_tensor(cur1[:, j % 2, :], f[:, 0:M], f[:, M:2 * M], ALU.add).then_inc(folds, 1)

            def batch_tile(bt, take=True, late=True, last=False):
                for q in range(QG):
                    for j in range(JT):
                        i = JT * q + j
                        if j == 1 and not (last and q == QG - 1):
                            spread(bt if q < QG - 1 else bt + 1, (q + 1) % QG)
                        if take and i == GATHER_FROM - 1:
                            pool.wait_ge(gathered, 16 * NF * (bt + 2))
                        if take and i == GATHER_FROM:
                            pool.wait_ge(ids_ready, bt + 3)
                            pool.wait_ge(rows_taken, bt + 2)
                        fold(bt, q, j)
                        if take and i == GATHER_FROM - 1:
                            take_ids(bt + 2)
                        if take and i >= GATHER_FROM:
                            gather(range(GATHERS * (i - GATHER_FROM), GATHERS * (i - GATHER_FROM + 1)))
                        if late and i * GATHERS + EARLY < NF:
                            gather(range(EARLY + GATHERS * i, min(EARLY + GATHERS * (i + 1), NF)))

            pool.wait_ge(ids_in, 16)
            take_ids(0)
            pool.wait_ge(ids_ready, 1)
            gather(range(NF))
            pool.wait_ge(gathered, 16 * NF)
            take_ids(1)
            pool.wait_ge(ids_ready, 2)
            pool.wait_ge(rows_taken, 1)
            gather(range(EARLY))
            pool.wait_ge(consts_made, 3)
            pool.wait_ge(ones_set, 1)
            pool.wait_ge(block_ready, 2)
            spread(0, 0)
            batch_tile(0)
            with pool.Fori(1, BT - 2) as bt:
                batch_tile(bt)
            batch_tile(BT - 2, take=False)
            batch_tile(BT - 1, take=False, late=False, last=True)

        @blk.scalar
        def _(act):
            lo = 0
            for i, hi in enumerate(f1_cuts):
                act.wait_ge(f1_in[i], 16)
                act.activation(f1_high[:, lo:hi, :].rearrange("p f m -> p (f m)"), f1_raw[:, lo * M:hi * M],
                               ACT.Copy).then_inc(f1_high_ready, 1)
                lo = hi
            for h in range(2):
                act.wait_ge(dense_filled, h + 1)
                act.activation(z_dense[:, h * 512:(h + 1) * 512], Y[h][0:D, :], ACT.Copy).then_inc(dense_read, 1)

            def take_rows(bt):
                act.wait_ge(gathered, 16 * NF * (bt + 1))
                if not (isinstance(bt, int) and bt == 0):
                    act.wait_ge(x_filled, FILLS * (bt - 1) + QG)
                by_dim = rows[:].rearrange("p (f d) -> p d f", d=D)
                act.activation(rows_seq[:, :, 0:SEL].rearrange("p d (j f) -> p d j f", f=NF),
                               by_dim.unsqueeze(2).broadcast_to([P, D, BLK, NF]), ACT.Copy)
                act.activation(rows_seq[:, :, SEL:SEQ], by_dim[:, :, 0:SEQ - SEL], ACT.Copy)\
                   .then_inc(rows_taken, 1)

            def read_transposes(bt, g):
                act.wait_ge(x_filled, FILLS * bt + g + 1)
                if g == 0 and not (isinstance(bt, int) and bt == 0):
                    for c in copied:
                        act.wait_ge(c, 16 * COPIES * (2 * bt))
                act.activation(x_seq[:, :, 4 * g:4 * g + 4],
                               X[g % 2][0:SEQ, :].rearrange("p (d b) -> p b d", d=4),
                               ACT.Copy).then_inc(x_read, 1)

            def read_scalars(bt, q):
                act.wait_ge(x_filled, FILLS * bt + QG + q + 1)
                if isinstance(bt, int) and bt == 0:
                    act.wait_ge(ones_set, 1)
                act.activation(x_col[:, q, :, 0:NF],
                               X[q % 2][:, 0:JT * 2 * NF].rearrange("p (j f) -> p j f", j=JT)[:, :, 0:NF],
                               ACT.Copy).then_inc(x_read, 1)

            def split_cur0(bt, q):
                act.wait_ge(cur0_summed, K0 * (QG * bt + q + 1))
                act.activation(cur0_high[:, q % 2, :], C[:], ACT.Copy).then_inc(cur0_high_ready, 1)

            def read_g(bt, q, j):
                t = column_tile(bt, q, j)
                act.wait_ge(g_filled, t + 1)
                half = G[:, bass.ds((bt % 2) * (FC * P), FC * P)].rearrange("p (f b) -> p f b", b=P)
                b0 = GB * q + TB * j
                act.activation(half[:, :, b0:b0 + TB], GP[:, 0:TB * FC].rearrange("p (b f) -> p f b", b=TB),
                               ACT.Copy).then_inc(g_read, 1)

            def scale_chunk(bt, q, j, c):
                t = column_tile(bt, q, j)
                n = SCALED.index(c)
                act.wait_ge(y_filled, CH * t + c + 1)
                if n == 0:
                    if not (isinstance(t, int) and t < 2):
                        act.wait_ge(folds, 3 * (t - 1))
                    dst = acc_s[:, j % 2, :]
                else:
                    back = n - PR
                    if back >= 1:
                        act.wait_ge(acc_steps, NST * t + STEP_DONE[SCALED[back]])
                    elif not (isinstance(t, int) and t == 0):
                        act.wait_ge(acc_steps, NST * (t - 1) + STEP_DONE[SCALED[back + NSC - 1]])
                    dst = scaled_sb[:, (n - 1) % PR, :]
                for i, f in enumerate(CH_F[c]):
                    ins = act.activation(dst[:, i * M:(i + 1) * M],
                                         Y[(SLOTS * q + CH * j + c) % YB][:, i * M:(i + 1) * M],
                                         ACT.Copy, scale=x_col[:, q, j, f:f + 1])
                ins.then_inc(scaled, 1)

            def group(bt, q, first=False, last=False):
                nbt, nq = (bt, q + 1) if q < QG - 1 else (bt + 1, 0)
                for s in range(SLOTS):
                    j, c = divmod(s, CH)
                    if not (isinstance(bt, int) and bt == BT - 1):
                        if q == 1 and s == AT_ROWS:
                            take_rows(bt + 1)
                        if q == 2 and s < QG:
                            read_transposes(bt + 1, s)
                    if s == AT_SCALARS and not (isinstance(bt, int) and bt == BT - 1 and q >= 2):
                        read_scalars(bt + q // 2, (q + 2) % QG)
                    if s == AT_SPLIT and not last:
                        split_cur0(nbt, nq)
                    if c == AT_GREAD and not (first and j == 0):
                        pj = (j - 1) % JT
                        pq = q if j else (q - 1) % QG
                        read_g(bt if j or q else bt - 1, pq, pj)
                    if c in SCALED:
                        scale_chunk(bt, q, j, c)

            take_rows(0)
            for g in range(QG):
                read_transposes(0, g)
            read_scalars(0, 0)
            read_scalars(0, 1)
            split_cur0(0, 0)
            for q in range(QG):
                group(0, q, first=q == 0)
            with act.Fori(1, BT - 1) as bt:
                for q in range(QG):
                    group(bt, q)
            for q in range(QG):
                group(BT - 1, q, last=q == QG - 1)

            def relu1(h):
                for m in range(4):
                    act.wait_ge(m1_filled, 4 * h + m + 1)
                    act.activation(h1[:, m, h * 512:(h + 1) * 512], Y[m][:], ACT.Relu,
                                   bias=b1_sb[:, m:m + 1]).then_inc(m1_read, 1)

            def relu2(h):
                for m in range(2):
                    act.wait_ge(m2_filled, 2 * h + m + 1)
                    if h:
                        act.wait_ge(m3_filled, 1)
                    act.activation(h2[:, m, :], X[m][:], ACT.Relu, bias=b2_sb[:, m:m + 1]).then_inc(m2_read, 1)

            def read_y(h):
                act.wait_ge(m3_filled, h + 1)
                act.activation(y[:, h * 512:(h + 1) * 512], GP[0:1, :], ACT.Copy).then_inc(m3_read, 1)

            act.wait_ge(mlp_in, 96)
            relu1(0)
            read_g(BT - 1, QG - 1, JT - 1)
            relu2(0)
            read_y(0)
            relu1(1)
            relu2(1)
            read_y(1)

        @blk.vector
        def _(dve):
            dve.memset(f0_mirror[0:NF, 0, :], 0.0).then_inc(mirror_zero, 1)
            dve.memset(x_col[:, :, :, NF:FC], 1.0).then_inc(ones_set, 1)
            lo = 0
            for i, hi in enumerate(f1_cuts):
                dve.wait_ge(f1_high_ready, i + 1)
                dve.tensor_tensor(f1_low[:, lo:hi, :].rearrange("p f m -> p (f m)"), f1_raw[:, lo * M:hi * M],
                                  f1_high[:, lo:hi, :].rearrange("p f m -> p (f m)").bitcast(F32),
                                  ALU.subtract).then_inc(f1_ready, 1)
                lo = hi

            def pair(bt, q, k):
                z = K0 * (QG * bt + q) + k
                if k == 0:
                    dve.wait_ge(copied[q % 2], 16 * COPIES * (2 * bt + q // 2 + 1))
                if not (isinstance(z, int) and z < 2):
                    dve.wait_ge(cur0_summed, z - 1)
                r = K0_ROWS[k]
                dve.tensor_tensor(pairs[0:r, (K0 * q + k) % 2, :], shifted[0:r, q % 2, 1 + k, :],
                                  shifted[0:r, q % 2, 0, :], ALU.mult).then_inc(pairs_ready, 1)

            def split_cur0(bt, q):
                g = QG * bt + q
                dve.wait_ge(cur0_high_ready, g + 1)
                dve.tensor_tensor(cur0_low[:, q % 2, :], C[:], cur0_high[:, q % 2, :].bitcast(F32),
                                  ALU.subtract).then_inc(cur0_ready, 1)
                dve.tensor_reduce(z0[:, bass.ds(P * bt + GB * q, GB)],
                                  C[:].rearrange("p (b d) -> p b d", d=D), AX.X, ALU.add).then_inc(cur0_read, 1)

            def layer2_read(bt, part):
                n = L2_PARTS * bt + part
                dve.wait_ge(l2_filled, n + 1)
                z = z2[:, bass.ds(P * bt, P)]
                if part == 0:
                    dve.tensor_copy(z, C[:, 0:P]).then_inc(l2_read, 1)
                else:
                    dve.wait_ge(l2_read, n)
                    dve.tensor_tensor(z, C[:, 0:P], z, ALU.add).then_inc(l2_read, 1)

            def copy_z1(bt):
                dve.wait_ge(g_read, TPB * (bt + 1))
                dve.tensor_copy(z1[:, bass.ds(P * bt, P)], G[:, bass.ds((bt % 2) * (FC * P) + NF * P, P)])\
                    .then_inc(z1_copied, 1)

            def step(bt, q, j, n):
                kind, c, i = STEPS[n]
                t = column_tile(bt, q, j)
                xs = x_col[:, q, j, :]
                if kind == "add":
                    if n == STEPS.index(("add", SCALED[1], 0)):
                        pass
                    else:
                        before = max(m for m in range(n) if STEPS[m][0] == "add")
                        dve.wait_ge(acc_steps, NST * t + before + 1)
                    dve.wait_ge(scaled, NSC * t + SCALED.index(c) + 1)
                    w = M * len(CH_F[c])
                    a = acc_s[:, j % 2, 0:w]
                    dve.tensor_tensor(a, a, scaled_sb[:, (SCALED.index(c) - 1) % PR, 0:w], ALU.add)\
                        .then_inc(acc_steps, 1)
                    return
                fused = [m for m in range(n) if STEPS[m][0] == "fuse"]
                f = CH_F[c][i]
                src = Y[(SLOTS * q + CH * j + c) % YB][:, i * M:(i + 1) * M]
                half = acc_f[:, j % 2, (len(fused) % 2) * M:(len(fused) % 2 + 1) * M]
                if i == 0:
                    dve.wait_ge(y_filled, CH * t + c + 1)
                if not fused and not (isinstance(t, int) and t < 2):
                    dve.wait_ge(folds, 3 * (t - 1))
                if len(fused) < 2:
                    dve.tensor_scalar(half, src, xs[:, f:f + 1], None, ALU.mult).then_inc(acc_steps, 1)
                else:
                    dve.wait_ge(acc_steps, NST * t + fused[-2] + 1)
                    dve.scalar_tensor_tensor(half, src, xs[:, f:f + 1], half, ALU.mult, ALU.add)\
                        .then_inc(acc_steps, 1)

            def group(bt, q, layer2=True, last=False):
                nbt, nq = (bt, q + 1) if q < QG - 1 else (bt + 1, 0)
                for s in range(SLOTS):
                    j, c = divmod(s, CH)
                    if layer2 and q and s == 5:
                        layer2_read(bt - 1, q - 1)
                    if layer2 and q == 1 and s == 7:
                        copy_z1(bt - 1)
                    if not last:
                        if s in AT_PAIR:
                            pair(nbt, nq, AT_PAIR.index(s))
                        if s == AT_SPLIT:
                            split_cur0(nbt, nq)
                    now = [n for n in range(NST) if STEPS[n][0] == "fuse" and STEPS[n][1] == c
                           or STEPS[n][0] == "add" and STEPS[n][1] == c - 1]
                    for n in now:
                        step(bt, q, j, n)

            dve.wait_ge(f0_in, 16 * len(pieces))
            dve.wait_ge(mirror_zero, 1)
            n = K0 - 1
            dve.tensor_tensor(f0_sum[:, 0:n, :], f0_sum[:, 0:n, :], f0_mirror[:, 0:n, :], ALU.add).then_inc(f0_ready, 1)
            r = K0_ROWS[n]
            dve.tensor_tensor(f0_sum[0:r, n, :], f0_sum[0:r, n, :], f0_mirror[0:r, n, :], ALU.add).then_inc(f0_ready, 1)
            for k in range(K0):
                pair(0, 0, k)
            split_cur0(0, 0)
            for q in range(QG):
                group(0, q, layer2=False)
            with dve.Fori(1, BT - 1) as bt:
                for q in range(QG):
                    group(bt, q)
            for q in range(QG):
                group(BT - 1, q, last=q == QG - 1)
            copy_z1(BT - 1)
            for part in range(L2_PARTS):
                layer2_read(BT - 1, part)

        @blk.tensor
        def _(pe):
            pe.wait_ge(consts_made, 3)
            pe.wait_ge(dense_in, 16)
            for t in range(BT):
                ins = pe.matmul(Y[t // 4][0:D, (t % 4) * P:(t % 4 + 1) * P], dense_sb[:, t, :], ident[:],
                                start=True, stop=True)
                if t % 4 == 3:
                    ins.then_inc(dense_filled, 1)

            def x_free(bt, n):
                if not (isinstance(bt, int) and bt == 0 and n < 2):
                    pe.wait_ge(x_read, FILLS * bt + n - 1)

            def transposes(bt, g):
                x_free(bt, g)
                pe.wait_ge(rows_taken, bt + 1)
                for i in range(4):
                    ins = pe.transpose(X[g % 2][0:SEQ, i * P:(i + 1) * P],
                                       rows_seq[:, 4 * g + i, :], ident[:])
                ins.then_inc(x_filled, 1)

            x_cols = x_seq[:].rearrange("p b d -> p (b d)")

            def scalars(bt, q):
                x_free(bt, QG + q)
                pe.wait_ge(x_read, FILLS * bt + QG)
                for j in range(JT):
                    ins = pe.transpose(X[q % 2][:, j * 2 * NF:(j + 1) * 2 * NF],
                                       x_cols[0:2 * NF, q * GN + j * P:q * GN + (j + 1) * P], ident[0:2 * NF, 0:2 * NF])
                ins.then_inc(x_filled, 1)

            def cur0_sum(bt, q, k, after_layer2):
                z = K0 * (QG * bt + q) + k
                pe.wait_ge(pairs_ready, z + 1)
                if k == 0:
                    if after_layer2 is not None:
                        pe.wait_ge(l2_read, after_layer2)
                    elif not (isinstance(bt, int) and QG * bt + q == 0):
                        pe.wait_ge(cur0_read, QG * bt + q)
                r = K0_ROWS[k]
                pe.matmul(C[:], f0_sum[0:r, k, :], pairs[0:r, (K0 * q + k) % 2, :],
                          start=k == 0, stop=k == K0 - 1).then_inc(cur0_summed, 1)

            def g_product(bt, q, j):
                t = column_tile(bt, q, j)
                pe.wait_ge(folds, 3 * (t + 1))
                pe.wait_ge(block_made, QG * bt + q + 1)
                if not (isinstance(t, int) and t == 0):
                    pe.wait_ge(g_read, t)
                pe.matmul(GP[:, 0:TB * FC], cur1[:, j % 2, :], x_block[:, q % 2, j, :],
                          start=True, stop=True).then_inc(g_filled, 1)

            def layer2(bt, part, fs):
                first, end = L2_F * part, L2_F * (part + 1)
                if fs[0] == first:
                    pe.wait_ge(g_read, TPB * (bt + 1))
                    pe.wait_ge(cur0_read, min(QG * (bt + 1) + part + 2, QG * BT) if isinstance(bt, int)
                               else QG * (bt + 1) + part + 2)
                    if bt is BT - 1 and part:
                        pe.wait_ge(l2_read, L2_PARTS * bt + part)
                for f in fs:
                    ins = pe.matmul(C[:, 0:P], f2_sb[:, f, :], G[:, bass.ds((bt % 2) * (FC * P) + f * P, P)],
                                    start=f == first, stop=f == end - 1)
                if fs[-1] == end - 1:
                    ins.then_inc(l2_filled, 1)

            def chunk(bt, q, j, c):
                t = column_tile(bt, q, j)
                if not (isinstance(t, int) and t == 0 and c < YB):
                    before, pc = (t, c - YB) if c >= YB else (t - 1, c - YB + CH)
                    if pc in FUSED:
                        pe.wait_ge(acc_steps, NST * before + STEP_DONE[pc])
                    else:
                        pe.wait_ge(scaled, NSC * before + SCALED.index(pc) + 1)
                bank = Y[(SLOTS * q + CH * j + c) % YB][:, 0:M * len(CH_F[c])]
                lo, hi = CH_F[c][0], CH_F[c][-1] + 1
                wh = f1_high[:, lo:hi, :].rearrange("p f m -> p (f m)")
                wl = f1_low[:, lo:hi, :].rearrange("p f m -> p (f m)")
                ch = cur0_high[:, q % 2, j * P:(j + 1) * P]
                cl = cur0_low[:, q % 2, j * P:(j + 1) * P]
                pe.matmul(bank, ch, wh, start=True, stop=False)
                pe.matmul(bank, ch, wl, start=False, stop=False)
                pe.matmul(bank, cl, wh, start=False, stop=True).then_inc(y_filled, 1)

            l2_slices = [range(0, 4), range(4, 7), range(7, 10), range(10, 13)]

            def group(bt, q, with_layer2=True, first=False, last=False):
                nbt, nq = (bt, q + 1) if q < QG - 1 else (bt + 1, 0)
                for s in range(SLOTS):
                    j, c = divmod(s, CH)
                    if s == 0:
                        pe.wait_ge(cur0_ready, QG * bt + q + 1)
                    if q == 2 and s < QG and not (isinstance(bt, int) and bt == BT - 1):
                        transposes(bt + 1, s)
                    if s == AT_SCALARS and not (isinstance(bt, int) and bt == BT - 1 and q >= 2):
                        scalars(bt + q // 2, (q + 2) % QG)
                    if s in AT_SUM and not last:
                        after = L2_PARTS * (bt - 1) + q if with_layer2 and q else None
                        cur0_sum(nbt, nq, AT_SUM.index(s), after)
                    if with_layer2 and q and s < 4:
                        layer2(bt - 1, q - 1, [L2_F * (q - 1) + f for f in l2_slices[s]])
                    if c == AT_G and not (first and j == 0):
                        pj = (j - 1) % JT
                        pq = q if j else (q - 1) % QG
                        g_product(bt if j or q else bt - 1, pq, pj)
                    chunk(bt, q, j, c)

            for g in range(QG):
                transposes(0, g)
            scalars(0, 0)
            scalars(0, 1)
            pe.wait_ge(f0_ready, 2)
            for k in range(K0):
                cur0_sum(0, 0, k, None)
            pe.wait_ge(f1_ready, len(f1_cuts))
            pe.wait_ge(dense_read, 2)
            pe.wait_ge(f2_in, 16)
            for q in range(QG):
                group(0, q, with_layer2=False, first=q == 0)
            with pe.Fori(1, BT - 1) as bt:
                for q in range(QG):
                    group(bt, q)
            for q in range(QG):
                group(BT - 1, q, last=q == QG - 1)

            def mlp1(h):
                for m in range(4):
                    if h:
                        pe.wait_ge(m1_read, m + 1)
                    for k, z in enumerate((z0, z1, z2)):
                        pe.matmul(Y[m][:], w1_sb[:, k, m * P:(m + 1) * P], z[:, h * 512:(h + 1) * 512],
                                  start=k == 0, stop=False)
                    pe.matmul(Y[m][:], w1_dense[:, m * P:(m + 1) * P], z_dense[:, h * 512:(h + 1) * 512],
                              start=False, stop=True).then_inc(m1_filled, 1)

            def mlp2(h):
                for m in range(2):
                    if h:
                        pe.wait_ge(m2_read, m + 1)
                    for k in range(4):
                        if m == 0:
                            pe.wait_ge(m1_read, 4 * h + k + 1)
                        ins = pe.matmul(X[m][:], w2_sb[:, k, m * P:(m + 1) * P], h1[:, k, h * 512:(h + 1) * 512],
                                        start=k == 0, stop=k == 3)
                    ins.then_inc(m2_filled, 1)

            def mlp3(h):
                if h:
                    pe.wait_ge(m3_read, 1)
                for k in range(2):
                    pe.wait_ge(m2_read, 2 * h + k + 1)
                    ins = pe.matmul(GP[0:1, :], w3_sb[:, k:k + 1], h2[:, k, :], start=k == 0, stop=k == 1)
                ins.then_inc(m3_filled, 1)

            pe.wait_ge(mlp_in, 96)
            pe.wait_ge(z1_copied, BT - 1)
            pe.wait_ge(l2_read, L2_PARTS * (BT - 1))
            pe.wait_ge(acc_steps, NST * TPB * BT)
            pe.wait_ge(scaled, NSC * TPB * BT)
            mlp1(0)
            g_product(BT - 1, QG - 1, JT - 1)
            mlp2(0)
            for part in range(L2_PARTS):
                layer2(BT - 1, part, [L2_F * part + f for f in range(L2_F)])
            mlp3(0)
            pe.wait_ge(z1_copied, BT)
            pe.wait_ge(l2_read, L2_PARTS * BT)
            mlp1(1)
            mlp2(1)
            mlp3(1)


_INS = (["dense_ctx", "ids"] + [f"tbl_{i}" for i in range(39)]
        + ["W_top1", "b_top1", "W_top2", "b_top2", "W_top3", "L0_rec_f0", "L0_rec_f1", "L0_rec_f2"])


def kernel(**inputs):
    import numpy as _np
    import concourse.bacc as _bacc
    from concourse import mybir as _mybir
    from concourse.bass_utils import run_bass_kernel_spmd as _run

    nc = _bacc.Bacc("TRN2", target_bir_lowering=False, num_devices=1)
    arrays, args = {}, {}
    for name in _INS:
        a = _np.ascontiguousarray(inputs[name])
        arrays[f"in_{name}_dram"] = a
        args[name] = nc.dram_tensor(f"in_{name}_dram", a.shape, _mybir.dt.from_np(a.dtype), kind="ExternalInput").ap()
    out = nc.dram_tensor("out_0_dram", (B, 1), _mybir.dt.float32, kind="ExternalOutput").ap()
    build(nc, args["dense_ctx"], args["ids"], [args[f"tbl_{i}"] for i in range(39)],
          args["W_top1"], args["b_top1"], args["W_top2"], args["b_top2"], args["W_top3"],
          args["L0_rec_f0"], args["L0_rec_f1"], args["L0_rec_f2"], out)
    r = _run(nc, [arrays], core_ids=[0])
    return r.results[0]["out_0_dram"]
```
